# Optimizing a Trainium2 kernel written in Bass

```python
import numpy as np
import jax
import jax.numpy as jnp

def _softmax(x, axis=-1):
    return jax.nn.softmax(x, axis=axis)

def _gelu(x):
    return jax.nn.gelu(x, approximate=True)

def _silu(x):
    return jax.nn.silu(x)

def _sigmoid(x):
    return jax.nn.sigmoid(x)

def _layernorm(x, axis=-1, eps=1e-05):
    m = jnp.mean(x, axis=axis, keepdims=True)
    v = jnp.var(x, axis=axis, keepdims=True)
    return (x - m) / jnp.sqrt(v + eps)

def _scatter_add(tgt, idx, src, axis=0):
    return tgt.at[idx].add(src)

def _segment_sum(src, seg, n):
    return jax.ops.segment_sum(src, seg, n)
kernel_name = 'mk_gnn_ffn_d1_gnn_r8_bdb844'

def setup_inputs(seed: int=0):
    np.random.seed(seed)
    _w = jnp.asarray

    def _rec_inputs():
        import jax
        import jax.numpy as jnp
        _gk = jax.random.key(seed)
        x = -0.0002117 + 1 * jax.random.normal(jax.random.fold_in(_gk, 1), (12500, 256), jnp.float32)
        src = jax.random.randint(jax.random.fold_in(_gk, 2), (200000,), 0, 12500, jnp.int32)
        dst = jnp.minimum((12500 * jax.random.uniform(jax.random.fold_in(_gk, 3), (200000,)) ** 2.0).astype(jnp.int32), 99999)
        _o = jnp.argsort(dst, stable=True)
        src = src[_o]
        dst = dst[_o]
        return (x, src, dst)
    x, src, dst = _rec_inputs()

    def _L0_gnn_setup():
        import jax, jax.numpy as jnp
        import numpy as np
        N_NODES = 12500
        N_EDGES = 200000
        D_IN = 256
        D_OUT = 256
        key = jax.random.key(seed)
        k1, k2, k3, k4, k5 = jax.random.split(key, 5)
        feat = jax.random.normal(k1, (N_NODES, D_IN), dtype=jnp.float32)
        lim = float(np.sqrt(6.0 / (D_IN + D_OUT)))
        W_neigh = jax.random.uniform(k2, (D_OUT, D_IN), minval=-lim, maxval=lim, dtype=jnp.float32)
        W_self = jax.random.uniform(k3, (D_OUT, D_IN), minval=-lim, maxval=lim, dtype=jnp.float32)
        b_self = jnp.zeros((D_OUT,), dtype=jnp.float32)
        src = jax.random.randint(k4, (N_EDGES,), 0, N_NODES, dtype=jnp.int32)
        dst = jax.random.randint(k5, (N_EDGES,), 0, N_NODES, dtype=jnp.int32)
        return {'feat': feat, 'W_neigh': W_neigh, 'W_self': W_self, 'b_self': b_self, 'src': src, 'dst': dst}
    _L0_gnn_all = _L0_gnn_setup()
    _L0_gnn_in = {k: v for k, v in _L0_gnn_all.items() if k in ('W_neigh', 'W_self', 'b_self')}
    del _L0_gnn_all

    def _L0_ffn_setup():
        import jax, jax.numpy as jnp
        import numpy as np
        E, D, H, TOP_K = (6, 256, 256, 2)
        ROUTER_H = D // 2
        key = jax.random.key(seed)
        ks = jax.random.split(key, 12)
        s = 1.0 / np.sqrt(D)
        sh = 1.0 / np.sqrt(H)
        sr = 1.0 / np.sqrt(ROUTER_H)
        return {'features': jax.random.normal(ks[0], (8, 512, D), dtype=jnp.float32), 'router_w1': jax.random.uniform(ks[1], (D, ROUTER_H), jnp.float32, -s, s), 'router_b1': jnp.zeros((ROUTER_H,), jnp.float32), 'router_w2': jax.random.uniform(ks[2], (ROUTER_H, E), jnp.float32, -sr, sr), 'router_b2': jnp.zeros((E,), jnp.float32), 'expert_w1': jax.random.uniform(ks[3], (E, D, H), jnp.float32, -s, s), 'expert_b1': jnp.zeros((E, H), jnp.float32), 'expert_w2': jax.random.uniform(ks[4], (E, H, H), jnp.float32, -sh, sh), 'expert_b2': jnp.zeros((E, H), jnp.float32), 'expert_w3': jax.random.uniform(ks[5], (E, H, D), jnp.float32, -sh, sh), 'expert_b3': jnp.zeros((E, D), jnp.float32)}
    _L0_ffn_all = _L0_ffn_setup()
    _L0_ffn_in = {k: v for k, v in _L0_ffn_all.items() if k in ('router_w1', 'router_b1', 'router_w2', 'router_b2', 'expert_w1', 'expert_b1', 'expert_w2', 'expert_b2', 'expert_w3', 'expert_b3')}
    del _L0_ffn_all
    return {'x': x, 'src': src, 'dst': dst, 'L0_gnn_W_neigh': _L0_gnn_in['W_neigh'], 'L0_gnn_W_self': _L0_gnn_in['W_self'], 'L0_gnn_b_self': _L0_gnn_in['b_self'], 'L0_ffn_router_w1': _L0_ffn_in['router_w1'], 'L0_ffn_router_b1': _L0_ffn_in['router_b1'], 'L0_ffn_router_w2': _L0_ffn_in['router_w2'], 'L0_ffn_router_b2': _L0_ffn_in['router_b2'], 'L0_ffn_expert_w1': _L0_ffn_in['expert_w1'], 'L0_ffn_expert_b1': _L0_ffn_in['expert_b1'], 'L0_ffn_expert_w2': _L0_ffn_in['expert_w2'], 'L0_ffn_expert_b2': _L0_ffn_in['expert_b2'], 'L0_ffn_expert_w3': _L0_ffn_in['expert_w3'], 'L0_ffn_expert_b3': _L0_ffn_in['expert_b3']}

def reference(x, src, dst, L0_gnn_W_neigh, L0_gnn_W_self, L0_gnn_b_self, L0_ffn_router_w1, L0_ffn_router_b1, L0_ffn_router_w2, L0_ffn_router_b2, L0_ffn_expert_w1, L0_ffn_expert_b1, L0_ffn_expert_w2, L0_ffn_expert_b2, L0_ffn_expert_w3, L0_ffn_expert_b3):
    import jax
    import jax.numpy as jnp

    def _L0_gnn_ref(feat, W_neigh, W_self, b_self, src, dst):
        import jax, jax.numpy as jnp
        import numpy as np
        N_NODES = 12500
        N_EDGES = 200000
        D_IN = 256
        D_OUT = 256
        msgs = feat[src]
        neigh_sum = jax.ops.segment_sum(msgs, dst, num_segments=N_NODES)
        deg = jax.ops.segment_sum(jnp.ones((src.shape[0],), dtype=feat.dtype), dst, num_segments=N_NODES)
        h_neigh = neigh_sum / jnp.maximum(deg, 1.0)[:, None]
        h_neigh = h_neigh @ W_neigh.T
        h_self = feat @ W_self.T + b_self
        return h_self + h_neigh

    def _L0_ffn_ref(features, router_w1, router_b1, router_w2, router_b2, expert_w1, expert_b1, expert_w2, expert_b2, expert_w3, expert_b3):
        import jax, jax.numpy as jnp
        import numpy as np
        E, D, H, TOP_K = (6, 256, 256, 2)
        ROUTER_H = D // 2
        rh = jax.nn.relu(features @ router_w1 + router_b1)
        expert_logits = jax.nn.softmax(rh @ router_w2 + router_b2, axis=-1)
        top_w, top_i = jax.lax.top_k(expert_logits, TOP_K)
        routing_weights = jax.nn.softmax(top_w, axis=-1)
        h1 = jax.nn.relu(jnp.einsum('bsd,edh->bseh', features, expert_w1) + expert_b1)
        h2 = jax.nn.relu(jnp.einsum('bseh,ehf->bsef', h1, expert_w2) + expert_b2)
        expert_out = jnp.einsum('bsef,efo->bseo', h2, expert_w3) + expert_b3
        sel = jnp.take_along_axis(expert_out, top_i[:, :, :, None], axis=2)
        combined = jnp.sum(sel * routing_weights[..., None], axis=2)
        return combined
    x = x + _L0_gnn_ref(_layernorm(x, axis=-1), L0_gnn_W_neigh, L0_gnn_W_self, L0_gnn_b_self, src, dst)
    x = x + _L0_ffn_ref(_layernorm(x, axis=-1)[None], L0_ffn_router_w1, L0_ffn_router_b1, L0_ffn_router_w2, L0_ffn_router_b2, L0_ffn_expert_w1, L0_ffn_expert_b1, L0_ffn_expert_w2, L0_ffn_expert_b2, L0_ffn_expert_w3, L0_ffn_expert_b3)[0]
    return x

_drawn_inputs = setup_inputs


def setup_inputs(seed=0):
    import zlib

    import numpy as np

    out = dict(_drawn_inputs(seed))
    spreads = {'L0_gnn_b_self': (0.0, 0.1),
     'L0_ffn_router_b1': (0.0, 0.3),
     'L0_ffn_router_b2': (0.0, 0.1),
     'L0_ffn_expert_b1': (0.0, 0.8),
     'L0_ffn_expert_b2': (0.0, 0.414),
     'L0_ffn_expert_b3': (0.0, 0.1)}
    factors = {}
    for name, (base, spread) in spreads.items():
        noise = np.random.default_rng([zlib.crc32(name.encode()), seed]).standard_normal(out[name].shape)
        drawn = base * np.exp(spread * noise) if base else spread * noise
        out[name] = jnp.asarray(drawn.astype(out[name].dtype))
    for name, factor in factors.items():
        out[name] = (out[name] * factor).astype(out[name].dtype)
    return out
```

```python
import math
from contextlib import ExitStack

import concourse.bass as bass
from concourse import mybir

ALU = mybir.AluOpType
ACT = mybir.ActivationFunctionType
AX_X = mybir.AxisListType.X
F32 = mybir.dt.float32
F16 = mybir.dt.float16
I32 = mybir.dt.int32
U32 = mybir.dt.uint32
U8 = mybir.dt.uint8

P = 128
N, D = 12500, 256
EDGES = 200000
EXPERTS = 6
KC = D // P
NT = -(-N // P)
ET = -(-EDGES // P)
OCT = 8
OCTS = -(-ET // OCT)
RING = 56
PART = 32
RING_OCTS = RING // OCT
LOOK = 16
BLOCKS = OCTS // RING_OCTS
ET_PAD = OCTS * OCT
ST = -(-ET_PAD // P)
OCT_ROWS = 104
OCT_COLS = ST * P // OCT // OCT_ROWS
STACK = 32
STACKED = 2 * STACK + EXPERTS
HOT = OCT // 2
LT = 7
LTURNS = NT // LT
HI_ACT = 3
FIRST, REST = slice(0, 4), slice(4, LT)
GROUPS = NT // 2
TOK = 2 * P
EPS = 1e-5
S_X = 1024.0
S_W = 1024.0
S_H = 16.0
ROW_BYTES = 2 * D * 2
DEG = TOK + 2 * EXPERTS


class Chain:

    def __init__(self, eng, sem, done):
        self.eng, self.sem, self.done, self.count = eng, sem, done, 0

    def link(self, ins):
        self.count += 1
        ins.then_inc(self.sem, 1)
        self.eng.wait_ge(self.sem, self.done + self.count)


def build(nc, x, src, dst, w_neigh, w_self, b_self, r_w1, r_b1, r_w2, r_b2,
          e_w1, e_b1, e_w2, e_b2, e_w3, e_b3, out):
    ctx = ExitStack()
    with ctx:
        def sb(name, shape, dt):
            return ctx.enter_context(nc.sbuf_tensor(name, shape, dt))

        def pb(name):
            return ctx.enter_context(nc.psum_tensor(name, [P, 512], F32))

        def sem(name):
            return ctx.enter_context(nc.semaphore(name))

        table = nc.dram_tensor("norm_table", (NT * P, 2 * D), F16, kind="Internal").ap()

        iota_f = sb("iota_f", [P, P], F32)
        iota_p = sb("iota_p", [P, 1], F32)
        iota_n128 = sb("iota_n128", [P, NT + 1], F32)
        ident = sb("ident", [P, P], F32)
        ident16 = sb("ident16", [P, P], F16)
        ones16 = sb("ones16", [P, P], F16)
        zero16 = sb("zero16", [P, P], F16)
        eps = sb("eps", [P, 1], F32)
        ln_scale = sb("ln_scale", [P, 1], F32)
        last_i = sb("last_i", [OCT_ROWS, OCT_COLS], I32)
        last_f = sb("last_f", [OCT_ROWS, OCT_COLS], F32)
        below = sb("below", [OCT_ROWS, OCT_COLS, NT + 1], F16)
        first_oct = sb("first_oct", [P, NT + 1], F32)
        turns_f = sb("turns_f", [P, GROUPS], F32)
        turns_i = sb("turns_i", [P, GROUPS], I32)
        dst_col = sb("dst_col", [P, ST * P], F32)
        idx = sb("idx", [P, ST * P], I32)
        idx_now = sb("idx_now", [P, RING], I32)
        stats = sb("stats", [P, LT, 6], F32)
        mv = sb("mv", [P, LT, 2], F32)
        lnv = sb("lnv", [P, LT], F32)
        guess = sb("guess", [P, LT], F32)
        newton = sb("newton", [P, 2, LT], F32)
        slope = sb("slope", [P, LT], F32)
        shift = sb("shift", [P, LT], F32)
        hl = sb("hl", [P, 2, LT, 2, D], F16)
        stage = sb("stage", [P, EXPERTS * KC, D], F32)
        gnn_w = sb("gnn_w", [P, 2, 2 * KC, D], F16)
        rw1 = sb("rw1", [P, 2, KC, P], F16)
        ew = [sb(f"ew{n}", [P, 2, EXPERTS * KC, D], F16) for n in (1, 2, 3)]
        rw2 = sb("rw2", [P, EXPERTS], F32)
        rw2_s = sb("rw2_s", [P, 2, EXPERTS], F16)
        rb1 = sb("rb1", [P, 1], F32)
        rb1_s = sb("rb1_s", [P, 1], F32)
        rb2 = sb("rb2", [P, EXPERTS], F32)
        bself = sb("bself", [P, D], F32)
        eb = sb("eb", [P, 2, EXPERTS * KC], F32)
        ebs = sb("ebs", [P, 2, EXPERTS * KC], F32)
        eb3 = sb("eb3", [STACKED, D], F32)
        eb3_s = sb("eb3_s", [STACKED, D], F16)
        rows = sb("rows", [P, RING * ROW_BYTES], U8)
        part = ST * P * 4
        dst_rows = rows[:, 0:part].bitcast(I32)
        src_rows = rows[:, part:2 * part].bitcast(I32)
        dstf_rows = rows[:, 2 * part:3 * part].bitcast(F32)
        srcf_rows = rows[:, 3 * part:4 * part].bitcast(F32)
        turns_part = 2 * LT * D * 4
        xin = rows[:, 4 * part:4 * part + turns_part].bitcast(F32).rearrange("p (i t d) -> p i t d", i=2, t=LT)
        xc = rows[:, 4 * part + turns_part:4 * part + 2 * turns_part].bitcast(F32).rearrange("p (i t d) -> p i t d", i=2, t=LT)
        ids = sb("ids", [P, 2, P], F32)
        hot = sb("hot", [P, 2, HOT, P], F16)
        rdeg = sb("rdeg", [P, 2], F32)
        agg = sb("agg", [P, 2, D], F32)
        x2 = sb("x2", [P, 2, D], F32)
        t2 = sb("t2", [P, 2, 2 * D], F16)
        xb = sb("xb", [P, 2, D], F32)
        tt = sb("tt", [P, 2, KC, TOK], F16)
        agg_t = sb("agg_t", [P, 2, KC, TOK], F16)
        h = sb("h", [P, 2, D], F32)
        stats2 = sb("stats2", [P, 2, 6], F32)
        mv2 = sb("mv2", [P, 2, 2], F32)
        lnv2 = sb("lnv2", [P, 2], F32)
        guess2 = sb("guess2", [P, 2], F32)
        newton2 = sb("newton2", [P, 2, 2], F32)
        rstd2 = sb("rstd2", [P, 2], F32)
        y = sb("y", [P, 2, D], F32)
        y_t = sb("y_t", [P, 2, KC, TOK], F16)
        rh = sb("rh", [P, TOK], F32)
        rh_s = sb("rh_s", [P, 2, TOK], F16)
        logit = sb("logit", [P, 2, EXPERTS], F32)
        top = sb("top", [P, 2], F32)
        expo = sb("expo", [P, 2, EXPERTS], F32)
        total = sb("total", [P, 2], F32)
        prob = sb("prob", [P, 2, 8], F32)
        best = sb("best", [P, 2, 8], F32)
        best_i = sb("best_i", [P, 2, 8], U32)
        best_f = sb("best_f", [P, 2, 8], F32)
        gap = sb("gap", [P, 2], F32)
        egap = sb("egap", [P, 2], F32)
        w12 = sb("w12", [P, 2, 2], F32)
        pick = sb("pick", [P, 2, 2, EXPERTS], F32)
        wsel = sb("wsel", [P, 2, EXPERTS], F32)
        wsel_s = sb("wsel_s", [P, 2, EXPERTS], F32)
        wsel_p = sb("wsel_p", [P, 2, STACKED], F16)
        wsel_t = sb("wsel_t", [STACKED, TOK], F16)
        t1 = sb("t1", [P, 2, KC, TOK], F32)
        tmp2 = sb("tmp2", [P, 2, KC, TOK], F32)
        h1 = sb("h1", [P, 2, 2, KC, TOK], F16)
        h2 = sb("h2", [P, 2, 2, KC, TOK], F16)
        acc = sb("acc", [P, 2, D], F32)

        seg = [pb("seg0"), pb("seg1")]
        bank_x, bank_y, bank_z = pb("bank_x"), pb("bank_y"), pb("bank_z")
        lay1, lay2, lay3 = pb("lay1"), pb("lay2"), pb("lay3")
        turn = [bank_x, bank_y]

        last_in = sem("last_in")
        iota_ok = sem("iota_ok")
        const_ok = sem("const_ok")
        below_ok = sem("below_ok")
        count_ok = sem("count_ok")
        bounds_ok = sem("bounds_ok")
        dst_in, src_in = sem("dst_in"), sem("src_in")
        conv_ok = sem("conv_ok")
        turned = sem("turned")
        copied = sem("copied")

        x_in = [[sem(f"x_in{i}_first"), sem(f"x_in{i}_rest")] for i in range(2)]
        stats_ok = sem("stats_ok")
        stats_seen = sem("stats_seen")
        var_ok = sem("var_ok")
        ln_ok = sem("ln_ok")
        guess_ok = sem("guess_ok")
        newton_chain = sem("newton_chain")
        affine_ok = sem("affine_ok")
        xc_first_ok, xc_ok = sem("xc_first_ok"), sem("xc_ok")
        hi_ok, hi_act_ok = sem("hi_ok"), sem("hi_act_ok")
        lo_ok = sem("lo_ok")
        table_out = [sem("table_out0"), sem("table_out1")]

        small_in = sem("small_in")
        stage_in = [sem(f"stage_in{n}") for n in range(4)]
        stage_hi = sem("stage_hi")
        stage_lo = sem("stage_lo")
        bias_ok = sem("bias_ok")
        small_lo = sem("small_lo")

        idx_ok = sem("idx_ok")
        granted = sem("granted")
        gathered = [sem(f"gathered{i}") for i in range(RING)]
        octs_ready = sem("octs_ready")
        free_octs = sem("free_octs")
        ids_ok = sem("ids_ok")
        hot_ready = [sem("hot_ready0"), sem("hot_ready1")]
        hot_free = [sem("hot_free0"), sem("hot_free1")]
        seg_done = sem("seg_done")
        deg_ok = sem("deg_ok")
        rdeg_ok = sem("rdeg_ok")
        aggh_scaled = sem("aggh_scaled")
        agg_ok = sem("agg_ok")

        x2_in, t2_in = sem("x2_in"), sem("t2_in")
        xb_ok = sem("xb_ok")
        tt_turned, tt_ok = sem("tt_turned"), sem("tt_ok")
        agg_turned, aggh_ok, aggl_ok = sem("agg_turned"), sem("aggh_ok"), sem("aggl_ok")
        gnn_done, h_ok = sem("gnn_done"), sem("h_ok")
        stats2_ok, var2_ok = sem("stats2_ok"), sem("var2_ok")
        ln2_ok, guess2_ok, newton2_chain = sem("ln2_ok"), sem("guess2_ok"), sem("newton2_chain")
        y_ok, y_turned, yh_ok, yl_ok = sem("y_ok"), sem("y_turned"), sem("yh_ok"), sem("yl_ok")
        rhh_ok, rhl_ok = sem("rhh_ok"), sem("rhl_ok")
        rh_done, rh_ok, logit_done = sem("rh_done"), sem("rh_ok"), sem("logit_done")
        route_chain = sem("route_chain")
        ws_ok = sem("ws_ok")
        shifted_ok, expo_ok, gap_ok, egap_ok, w_ok = (sem("shifted_ok"), sem("expo_ok"), sem("gap_ok"),
                                                      sem("egap_ok"), sem("w_ok"))
        wt_turned, wt_ok, b3_done, acc0_ok = sem("wt_turned"), sem("wt_ok"), sem("b3_done"), sem("acc0_ok")
        l1_done, t1_ok, h1h_ok, h1l_ok = sem("l1_done"), sem("t1_ok"), sem("h1h_ok"), sem("h1l_ok")
        l2_done, t2_ok, h2h_ok, h2l_ok = sem("l2_done"), sem("t2_ok"), sem("h2h_ok"), sem("h2l_ok")
        l3_done, acc_ok = sem("l3_done"), sem("acc_ok")
        out_done = sem("out_done")

        block = ctx.enter_context(nc.Block())

        table_turns = table.rearrange("(c t p) d -> c p t d", p=P, t=LT)
        x_turns = x.rearrange("(c t p) d -> c p t d", p=P, t=LT)

        def turns_of(eng, g):
            word = eng.value_load(turns_i[0:1, bass.ds(g, 1)])
            parts = (word & 255, (word >> 8) & 255, word >> 16)
            return [eng.snap(part).with_bounds(min_val=0, max_val=OCTS - 1) for part in parts]

        def one(ap, k):
            return ap[bass.ds(k, 1)].rearrange("a p t d -> p (a t) d")

        def row(start):
            return rows[:, bass.ds(start, ROW_BYTES)].bitcast(F16)

        @block.sync
        def _(sp):
            with nc.allow_non_contiguous_dma("one element per edge tile; columns of biases"):
                sp.dma_start(last_i[:, :], dst.rearrange("(t p r) e -> p t r e", p=OCT_ROWS, r=OCT)[:, :, OCT - 1, P - 1]).then_inc(last_in, 16)
                def load_x(turn_rows, i, part):
                    sp.dma_start(xin[:, i, part], turn_rows[:, part]).then_inc(x_in[i][part is REST], 16)

                for i in range(2):
                    for part in (FIRST, REST):
                        load_x(x_turns[i], i, part)
                sp.dma_start(dst_rows.rearrange("p (t e) -> p t e", t=ST), dst.rearrange("(t p) e -> p t e", p=P)).then_inc(dst_in, 16)
                sp.dma_start(src_rows.rearrange("p (t e) -> p t e", t=ST), src.rearrange("(t p) e -> p t e", p=P)).then_inc(src_in, 16)
                with sp.Fori(1, LTURNS // 2) as b:
                    for i in range(2):
                        for part, normalised in ((FIRST, xc_first_ok), (REST, xc_ok)):
                            sp.wait_ge(normalised, b * 2 + (i - 1))
                            load_x(one(x_turns, b * 2 + i), i, part)
                sp.dma_start(rw2[:, :], r_w2).then_inc(small_in, 16)
                sp.dma_start(rb1[:, :], r_b1.rearrange("(p a) -> p a", a=1)).then_inc(small_in, 16)
                sp.dma_start(rb2[:, :], r_b2.partition_broadcast(P)).then_inc(small_in, 16)
                sp.dma_start(bself[:, :], b_self.partition_broadcast(P)).then_inc(small_in, 16)
                for n, b_e in enumerate((e_b1, e_b2)):
                    sp.dma_start(eb[:, n], b_e.rearrange("e (m p) -> p (e m)", p=P)).then_inc(small_in, 16)
                for n in range(3):
                    sp.dma_start(eb3[n * STACK:n * STACK + EXPERTS, :], e_b3).then_inc(small_in, 16)
                sp.dma_start(stage[:, 0:KC], w_neigh.rearrange("(k p) o -> p k o", p=P)).then_inc(stage_in[0], 16)
                sp.dma_start(stage[:, KC:2 * KC], w_self.rearrange("(k p) o -> p k o", p=P)).then_inc(stage_in[0], 16)
                sp.dma_start(stage[:, 2 * KC:3 * KC, 0:P], r_w1.rearrange("(k p) o -> p k o", p=P)).then_inc(stage_in[0], 16)
                for n, w_e in enumerate((e_w1, e_w2, e_w3)):
                    sp.wait_ge(stage_lo, 2 + n)
                    sp.dma_start(stage[:, :, :], w_e.rearrange("e (k p) o -> p (e k) o", p=P)).then_inc(stage_in[n + 1], 16)
            with sp.Fori(1, BLOCKS + 1) as b:
                landed = sp.snap(b * 16)
                for r in range(RING):
                    sp.wait_ge(gathered[r], landed)
                    if r % OCT == OCT - 1:
                        sp.sem_inc(octs_ready, 1)

        @block.gpsimd
        def _(pool):
            def iota(to, pattern, per_partition):
                nc.gpsimd.iota(to[:, :], pattern, base=0, channel_multiplier=per_partition,
                               allow_small_or_imprecise_dtypes=True).then_inc(iota_ok, 1)

            iota(iota_f, [[1, P]], 0)
            iota(iota_p, [[0, 1]], 1)
            iota(iota_n128, [[P, NT + 1]], 0)
            pool.wait_ge(dst_in, 16)
            nc.gpsimd.tensor_copy(dstf_rows, dst_rows).then_inc(conv_ok, 1)
            pool.wait_ge(src_in, 16)
            nc.gpsimd.tensor_copy(srcf_rows, src_rows).then_inc(conv_ok, 1)
            with pool.Fori(0, LTURNS // 2) as b:
                for i in range(2):
                    pool.wait_ge(hi_ok, b * 2 + (i + 1))
                    pool.wait_ge(hi_act_ok, b * 2 + (i + 1))
                    nc.gpsimd.tensor_tensor(hl[:, i, :, 1, :], xc[:, i, :, :], hl[:, i, :, 0, :], ALU.subtract).then_inc(lo_ok, 1)
            pool.wait_ge(copied, 2 * -(-ST // 4))
            for i in range(2):
                pool.wait_ge(table_out[i], 16 * LTURNS // 2)
            nc.gpsimd.tensor_copy(idx_now[:, 0:PART], idx[:, 0:PART]).then_inc(idx_ok, 1)

            def turn_of_ring(b):
                for r in range(RING):
                    if r == LOOK:
                        if not (isinstance(b, int) and b == 0):
                            pool.wait_ge(octs_ready, b * RING_OCTS)
                        nc.gpsimd.tensor_copy(idx_now[:, PART:RING], idx[:, bass.ds(b * RING + PART, RING - PART)]).then_inc(idx_ok, 1)
                    if r == PART + LOOK and not isinstance(b, int):
                        next_part(b)
                    if r == PART + LOOK and isinstance(b, int) and b < BLOCKS - 1:
                        next_part(b)
                    if r == 0:
                        pool.wait_ge(idx_ok, b * 2 + 1)
                        pool.sem_inc(granted, 1)
                    if r == PART:
                        pool.wait_ge(idx_ok, b * 2 + 2)
                        pool.sem_inc(granted, 1)
                    if r % OCT == 0:
                        pool.wait_ge(free_octs, b * RING_OCTS + (r // OCT + 1))
                        pool.sem_inc(granted, 1)
                    nc.gpsimd.indirect_dma_start(out=row(r * ROW_BYTES), out_offset=None, in_=table,
                                                 in_offset=bass.IndirectOffsetOnAxis(ap=idx_now[:, r:r + 1], axis=0)).then_inc(gathered[r], 16)

            def next_part(b):
                pool.wait_ge(octs_ready, b * RING_OCTS + PART // OCT)
                nc.gpsimd.tensor_copy(idx_now[:, 0:PART], idx[:, bass.ds(b * RING + RING, PART)]).then_inc(idx_ok, 1)

            turn_of_ring(0)
            with pool.Fori(1, BLOCKS - 1) as b:
                turn_of_ring(b)
            turn_of_ring(BLOCKS - 1)
            pool.wait_ge(octs_ready, OCTS)

        @block.scalar
        def _(act):
            act.wait_ge(const_ok, 9)
            nc.scalar.preload_act_table_set("natural_log_exp_and_others")

            def store(b, i):
                act.wait_ge(lo_ok, b * 2 + (i + 1))
                act.dma_start(one(table_turns, b * 2 + i), hl[:, i].rearrange("p t h d -> p t (h d)")).then_inc(table_out[i], 16)

            def norm_turn(b, i):
                k = b * 2 + (i + 1)
                act.wait_ge(var_ok, k)
                nc.scalar.activation(lnv[:, :], mv[:, :, 1], ACT.Ln, bias=eps[:, :]).then_inc(ln_ok, 1)
                act.wait_ge(ln_ok, k)
                nc.scalar.activation(guess[:, :], lnv[:, :], ACT.Exp, bias=ln_scale[:, :], scale=-0.5).then_inc(guess_ok, 1)
                static = isinstance(b, int)
                if not (static and b == 0):
                    store(b - 1, i)
                act.wait_ge(affine_ok, k)
                for t in range(LT):
                    ins = nc.scalar.activation(xc[:, i, t, :], xin[:, i, t, :], ACT.Identity, scale=slope[:, t:t + 1], bias=shift[:, t:t + 1])
                    if t == FIRST.stop - 1:
                        ins.then_inc(xc_first_ok, 1)
                ins.then_inc(xc_ok, 1)
                act.wait_ge(xc_ok, k)
                if not (static and b == 0):
                    act.wait_ge(table_out[i], b * 16)
                nc.scalar.copy(hl[:, i, 0:HI_ACT, 0, :], xc[:, i, 0:HI_ACT, :]).then_inc(hi_act_ok, 1)

            norm_turn(0, 0)
            norm_turn(0, 1)
            n = 0
            for to in (dst_col, idx):
                for q in range(0, ST, 4):
                    w = min(4, ST - q)
                    act.wait_ge(turned, n + 1)
                    nc.scalar.copy(to[:, q * P:(q + w) * P], turn[n % 2][:, 0:w * P]).then_inc(copied, 1)
                    n += 1

            with act.Fori(1, LTURNS // 2) as b:
                norm_turn(b, 0)
                norm_turn(b, 1)
            for i in range(2):
                store(LTURNS // 2 - 1, i)

            def high(n, to, frm):
                act.wait_ge(stage_in[n], 48 if n == 0 else 16)
                nc.scalar.activation(to, frm, ACT.Copy, scale=S_W).then_inc(stage_hi, 1)

            high(0, gnn_w[:, 0], stage[:, 0:2 * KC])
            high(0, rw1[:, 0], stage[:, 2 * KC:3 * KC, 0:P])
            for n in range(3):
                high(n + 1, ew[n][:, 0], stage[:, :, :])
            act.wait_ge(small_in, 16 * 9)
            nc.scalar.activation(ebs[:, :, :], eb[:, :, :], ACT.Copy, scale=S_H).then_inc(bias_ok, 1)
            nc.scalar.activation(rb1_s[:, :], rb1[:, :], ACT.Copy, scale=S_H).then_inc(bias_ok, 1)
            nc.scalar.activation(rw2_s[:, 0, :], rw2[:, :], ACT.Copy, scale=S_W).then_inc(bias_ok, 1)
            for n in range(3):
                at = slice(n * STACK, n * STACK + EXPERTS)
                nc.scalar.activation(eb3_s[at, :], eb3[at, :], ACT.Copy, scale=S_W).then_inc(bias_ok, 1)
            act.wait_ge(bias_ok, 6)

            def load_group(g):
                act.dma_start(x2[:, :, :], x.rearrange("(t p) d -> p t d", p=P)[:, bass.ds(g * 2, 2), :]).then_inc(x2_in, 16)
                act.dma_start(t2[:, :, :], table.rearrange("(t p) d -> p t d", p=P)[:, bass.ds(g * 2, 2), :]).then_inc(t2_in, 16)

            def iteration(g, front, ffn, more):
                g1 = g + 1 if isinstance(g, int) else act.snap(g + 1)
                f6 = (g - 1) * EXPERTS if isinstance(g, int) else act.snap((g - 1) * EXPERTS)

                def hidden(e, done, bank, tmp, tmp_ok, hid, hid_ok, bias, scale):
                    act.wait_ge(done, f6 + (e + 1))
                    for m in range(KC):
                        c = e % EXPERTS * KC + m
                        ins = nc.scalar.activation(tmp[:, e % 2, m], bank[:, m * TOK:(m + 1) * TOK], ACT.Relu,
                                                   bias=ebs[:, bias, c:c + 1], scale=scale)
                    ins.then_inc(tmp_ok, 1)
                    act.wait_ge(tmp_ok, f6 + (e + 1))
                    nc.scalar.copy(hid[:, e % 2, 0], tmp[:, e % 2]).then_inc(hid_ok, 1)

                def hidden1(e):
                    if ffn or e == EXPERTS:
                        hidden(e, l1_done, lay1, t1, t1_ok, h1, h1h_ok, 0, S_H / (S_X * S_W))

                def hidden2(e):
                    if ffn:
                        hidden(e, l2_done, lay2, tmp2, t2_ok, h2, h2h_ok, 1, 1.0 / S_W)

                if front:
                    act.wait_ge(rdeg_ok, g1)
                    for j in range(2):
                        nc.scalar.activation(agg[:, j, :], seg[j][:, 0:D], ACT.Identity, scale=rdeg[:, j:j + 1]).then_inc(aggh_scaled, 1)
                hidden1(1)
                if ffn:
                    act.wait_ge(wt_turned, g)
                    nc.scalar.copy(wsel_t[:, :], bank_z[:, :].bitcast(F16)[0:STACKED, 0:TOK]).then_inc(wt_ok, 1)
                if front:
                    act.wait_ge(agg_turned, g1)
                    nc.scalar.copy(agg_t[:, 0].rearrange("p k t -> p (k t)"), bank_y[:, :]).then_inc(aggh_ok, 1)
                    act.wait_ge(tt_turned, g1)
                    nc.scalar.copy(tt[:, :, :, :].rearrange("p h k t -> p (h k t)"), bank_x[:, :].bitcast(F16)).then_inc(tt_ok, 1)
                hidden2(0)
                hidden1(2)
                hidden2(1)
                hidden1(3)
                if front:
                    act.wait_ge(var2_ok, g1)
                    nc.scalar.activation(lnv2[:, :], mv2[:, :, 1], ACT.Ln, bias=eps[:, :]).then_inc(ln2_ok, 1)
                    act.wait_ge(ln2_ok, g1)
                    nc.scalar.activation(guess2[:, :], lnv2[:, :], ACT.Exp, bias=ln_scale[:, :], scale=-0.5).then_inc(guess2_ok, 1)
                hidden2(2)
                hidden1(4)
                hidden2(3)
                hidden1(5)
                if front:
                    act.wait_ge(y_turned, g1)
                    nc.scalar.copy(y_t[:, 0].rearrange("p k t -> p (k t)"), bank_y[:, :]).then_inc(yh_ok, 1)
                hidden2(4)
                if front:
                    act.wait_ge(rh_done, g1)
                    nc.scalar.activation(rh[:, :], bank_x[:, 0:TOK], ACT.Relu, bias=rb1_s[:, 0:1], scale=S_H / (S_X * S_W)).then_inc(rh_ok, 1)
                    act.wait_ge(rh_ok, g1)
                    nc.scalar.copy(rh_s[:, 0, :], rh[:, :]).then_inc(rhh_ok, 1)
                hidden2(5)
                if front:
                    act.wait_ge(shifted_ok, g1)
                    nc.scalar.activation(expo[:, :, :], logit[:, :, :], ACT.Exp).then_inc(expo_ok, 1)
                if more:
                    act.wait_ge(xb_ok, g1)
                    load_group(g + 1)
                if front:
                    act.wait_ge(gap_ok, g1)
                    nc.scalar.activation(egap[:, :], gap[:, :], ACT.Exp).then_inc(egap_ok, 1)
                    hidden1(EXPERTS)
                if ffn:
                    act.wait_ge(acc_ok, f6 + EXPERTS)
                    act.dma_start(out.rearrange("(t p) d -> p t d", p=P)[:, bass.ds(g * 2 - 2, 2), :], acc[:, :, :]).then_inc(out_done, 16)
                    act.wait_ge(out_done, g * 16)

            load_group(0)
            iteration(0, True, False, True)
            with act.Fori(1, GROUPS - 1) as g:
                iteration(g, True, True, True)
            iteration(GROUPS - 1, True, True, False)
            iteration(GROUPS, False, True, False)

        @block.tensor
        def _(pe):
            pe.wait_ge(const_ok, 9)
            for t in range(OCT_COLS):
                pe.wait_ge(below_ok, t + 1)
                mm = pe.matmul(turn[0][:, 0:NT + 1], ones16[0:OCT_ROWS, :], below[:, t, :], start=(t == 0), stop=(t == OCT_COLS - 1))
            mm.then_inc(count_ok, 1)
            pe.wait_ge(bounds_ok, 1)
            n = 0
            for k, table_rows in enumerate((dstf_rows, srcf_rows)):
                pe.wait_ge(conv_ok, k + 1)
                for q in range(0, ST, 4):
                    if n >= 2:
                        pe.wait_ge(copied, n - 1)
                    for t in range(min(4, ST - q)):
                        mm = pe.transpose(turn[n % 2][:, t * P:(t + 1) * P], table_rows[:, (q + t) * P:(q + t + 1) * P], ident[:, :])
                    mm.then_inc(turned, 1)
                    n += 1
            pe.wait_ge(copied, n)
            pe.wait_ge(bounds_ok, 5)
            pe.sem_inc(free_octs, RING_OCTS)
            for half in range(2):
                pe.sem_inc(hot_free[half], 1)

            def exact(out_ap, stationary, moving, first, last):
                n = len(stationary)
                for k in range(n):
                    (sh, sl), (mh, ml) = stationary[k], moving[k]
                    pe.matmul(out_ap, sh, mh, start=(first and k == 0), stop=False)
                    pe.matmul(out_ap, sh, ml, start=False, stop=False)
                    mm = pe.matmul(out_ap, sl, mh, start=False, stop=(last and k == n - 1))
                return mm

            def visit(n1, j, q, first):
                v1 = pe.snap(q + n1)
                start = pe.snap((q % RING_OCTS) * (OCT * ROW_BYTES))
                pe.wait_ge(octs_ready, pe.snap(q + 1))
                for half in range(2):
                    pe.wait_ge(hot_ready[half], v1)
                    for i in range(HOT):
                        w = hot[:, half, i, :]
                        mm = pe.matmul(seg[j][:, :], w, row(start + (half * HOT + i) * ROW_BYTES), start=(first and half == 0 and i == 0),
                                       stop=False, skip_group_check=True)
                        if not first and half == 0 and i == 0:
                            mm.then_inc(free_octs, 1)
                        mm = pe.matmul(bank_x[:, DEG + j:DEG + j + 1], w, ones16[:, 0:1], start=False, stop=False, skip_group_check=True)
                    mm.then_inc(hot_free[half], 1)

            def visits(g, j, first_q, last_q):
                n1 = g * 2 + (j + 1)
                if not isinstance(n1, int):
                    n1 = pe.snap(n1)
                visit(n1, j, first_q, True)
                with pe.If(first_q < last_q):
                    with pe.Fori(first_q + 1, last_q + 1) as q:
                        visit(n1, j, q, False)
                pe.matmul(bank_x[:, DEG + j:DEG + j + 1], zero16[:, :], ones16[:, 0:1], start=False, stop=True, skip_group_check=True)
                pe.matmul(seg[j][:, 0:1], zero16[:, :], ones16[:, 0:1], start=False, stop=True, skip_group_check=True).then_inc(seg_done, 1)

            def open_counts():
                pe.matmul(bank_x[:, DEG:DEG + 2], zero16[:, :], ones16[:, 0:2], start=True, stop=False, skip_group_check=True)

            def iteration(g, front, ffn, more):
                g1 = g + 1 if isinstance(g, int) else pe.snap(g + 1)
                f6 = (g - 1) * EXPERTS if isinstance(g, int) else pe.snap((g - 1) * EXPERTS)

                def layer(e, bank, w, act_in):
                    for m in range(KC):
                        mm = exact(bank[:, m * TOK:(m + 1) * TOK],
                                   [(w[:, 0, e * KC + k, m * P:(m + 1) * P], w[:, 1, e * KC + k, m * P:(m + 1) * P]) for k in range(KC)],
                                   [(act_in[:, 0, k, :], act_in[:, 1, k, :]) for k in range(KC)], True, True)
                    return mm

                def layer1(e):
                    if ffn:
                        pe.wait_ge(t1_ok, f6 + e)
                        layer(e, lay1, ew[0], y_t).then_inc(l1_done, 1)

                def layer2(e):
                    if ffn:
                        if e:
                            pe.wait_ge(t2_ok, f6 + e)
                        pe.wait_ge(h1h_ok, f6 + (e + 1))
                        pe.wait_ge(h1l_ok, f6 + (e + 1))
                        layer(e, lay2, ew[1], h1[:, e % 2]).then_inc(l2_done, 1)

                def layer3(e):
                    if ffn:
                        if e:
                            pe.wait_ge(acc_ok, f6 + e)
                        pe.wait_ge(h2h_ok, f6 + (e + 1))
                        pe.wait_ge(h2l_ok, f6 + (e + 1))
                        for j in range(2):
                            mm = exact(lay3[:, j * D:(j + 1) * D],
                                       [(h2[:, e % 2, 0, k, j * P:(j + 1) * P], h2[:, e % 2, 1, k, j * P:(j + 1) * P]) for k in range(KC)],
                                       [(ew[2][:, 0, e * KC + k, :], ew[2][:, 1, e * KC + k, :]) for k in range(KC)], True, True)
                        mm.then_inc(l3_done, 1)

                layer1(1)
                layer2(0)
                if ffn:
                    pe.wait_ge(w_ok, g)
                    for j in range(2):
                        mm = pe.transpose(bank_z[:, :].bitcast(F16)[0:STACKED, j * P:(j + 1) * P], wsel_p[:, j, :], ident16[:, :])
                    mm.then_inc(wt_turned, 1)
                if front:
                    pe.wait_ge(t2_in, g1 * 16)
                    pe.wait_ge(rdeg_ok, g1)
                    for part in range(2):
                        for k in range(KC):
                            for j in range(2):
                                at = ((part * KC + k) * 2 + j) * P
                                c = part * D + k * P
                                mm = pe.transpose(bank_x[:, :].bitcast(F16)[:, at:at + P], t2[:, j, c:c + P], ident16[:, :])
                    mm.then_inc(tt_turned, 1)
                if front:
                    pe.wait_ge(agg_ok, g1 * 2)
                    for k in range(KC):
                        for j in range(2):
                            at = (k * 2 + j) * P
                            mm = pe.transpose(bank_y[:, at:at + P], agg[:, j, k * P:(k + 1) * P], ident[:, :])
                    mm.then_inc(agg_turned, 1)
                if ffn:
                    pe.wait_ge(wt_ok, g)
                    for j in range(2):
                        mm = pe.matmul(bank_z[:, j * D:(j + 1) * D], wsel_t[:, j * P:(j + 1) * P], eb3_s[:, :], start=True, stop=True)
                    mm.then_inc(b3_done, 1)
                layer1(2)
                if front:
                    pe.wait_ge(aggh_ok, g1)
                    pe.wait_ge(aggl_ok, g1)
                    if ffn:
                        pe.wait_ge(acc0_ok, g)
                    for j in range(2):
                        to = bank_z[:, j * D:(j + 1) * D]
                        for n, part in enumerate((agg_t, tt)):
                            if j == 0 and n == 1:
                                pe.wait_ge(tt_ok, g1)
                            mm = exact(to, [(part[:, 0, k, j * P:(j + 1) * P], part[:, 1, k, j * P:(j + 1) * P]) for k in range(KC)],
                                       [(gnn_w[:, 0, n * KC + k, :], gnn_w[:, 1, n * KC + k, :]) for k in range(KC)], n == 0, n == 1)
                    mm.then_inc(gnn_done, 1)
                layer2(1)
                layer3(0)
                layer1(3)
                layer2(2)
                layer3(1)
                layer1(4)
                layer2(3)
                layer1(5)
                if front:
                    pe.wait_ge(y_ok, g1)
                    for k in range(KC):
                        for j in range(2):
                            at = (k * 2 + j) * P
                            mm = pe.transpose(bank_y[:, at:at + P], y[:, j, k * P:(k + 1) * P], ident[:, :])
                    mm.then_inc(y_turned, 1)
                layer3(2)
                layer2(4)
                if front:
                    pe.wait_ge(yh_ok, g1)
                    pe.wait_ge(yl_ok, g1)
                    exact(bank_x[:, 0:TOK], [(rw1[:, 0, k, :], rw1[:, 1, k, :]) for k in range(KC)],
                          [(y_t[:, 0, k, :], y_t[:, 1, k, :]) for k in range(KC)], True, True).then_inc(rh_done, 1)
                layer3(3)
                if more:
                    turns = turns_of(pe, g + 1)
                layer2(5)
                if front:
                    pe.wait_ge(rhh_ok, g1)
                    pe.wait_ge(rhl_ok, g1)
                    for j in range(2):
                        at = TOK + j * EXPERTS
                        mm = exact(bank_x[:, at:at + EXPERTS], [(rh_s[:, 0, j * P:(j + 1) * P], rh_s[:, 1, j * P:(j + 1) * P])],
                                   [(rw2_s[:, 0, :], rw2_s[:, 1, :])], True, True)
                    mm.then_inc(logit_done, 1)
                layer3(4)
                if more:
                    pe.wait_ge(shifted_ok, g1)
                    open_counts()
                    visits(g + 1, 0, turns[0], turns[1])
                layer3(5)
                if front:
                    if ffn:
                        pe.wait_ge(t1_ok, f6 + EXPERTS)
                    layer(0, lay1, ew[0], y_t).then_inc(l1_done, 1)
                if more:
                    visits(g + 1, 1, turns[1], turns[2])

            open_counts()
            turns = turns_of(pe, 0)
            for j in range(2):
                visits(0, j, turns[j], turns[j + 1])
            pe.wait_ge(stage_lo, 5)
            pe.wait_ge(small_lo, 2)
            iteration(0, True, False, True)
            with pe.Fori(1, GROUPS - 1) as g:
                iteration(g, True, True, True)
            iteration(GROUPS - 1, True, True, False)
            iteration(GROUPS, False, True, False)

        @block.vector
        def _(dve):
            V = nc.vector
            V.memset(ones16[:, :], 1.0).then_inc(const_ok, 1)
            V.memset(zero16[:, :], 0.0).then_inc(const_ok, 1)
            V.memset(eps[:, :], EPS).then_inc(const_ok, 1)
            V.memset(ln_scale[:, :], math.log(S_X)).then_inc(const_ok, 1)
            V.memset(prob[:, :, :], -1.0).then_inc(const_ok, 1)
            V.memset(eb3_s[:, :], 0.0).then_inc(const_ok, 1)
            V.memset(wsel_p[:, :, :], 0.0).then_inc(const_ok, 1)
            dve.wait_ge(iota_ok, 3)
            V.tensor_scalar(ident[:, :], iota_f[:, :], iota_p[:, 0:1], None, ALU.is_equal).then_inc(const_ok, 1)
            V.tensor_scalar(ident16[:, :], iota_f[:, :], iota_p[:, 0:1], None, ALU.is_equal).then_inc(const_ok, 1)
            dve.wait_ge(last_in, 16)
            V.tensor_copy(last_f[:, :], last_i[:, :]).then_inc(const_ok, 1)
            dve.wait_ge(const_ok, 10)
            for t in range(OCT_COLS):
                V.tensor_scalar(below[:, t, :], iota_n128[0:OCT_ROWS, :], last_f[:, t:t + 1], None, ALU.is_gt).then_inc(below_ok, 1)
            for j in range(2):
                V.tensor_scalar(ids[:, j, :], iota_f[:, :], float(j * P), None, ALU.add).then_inc(ids_ok, 1)
            dve.wait_ge(ids_ok, 2)
            dve.wait_ge(count_ok, 1)
            V.tensor_copy(first_oct[:, :], turn[0][:, 0:NT + 1]).then_inc(bounds_ok, 1)
            dve.wait_ge(bounds_ok, 1)
            V.memset(first_oct[:, NT:NT + 1], OCTS - 1).then_inc(bounds_ok, 1)
            dve.wait_ge(bounds_ok, 2)
            octs_by_tile = first_oct[:, 0:NT].rearrange("p (g j) -> p g j", j=2)
            V.scalar_tensor_tensor(turns_f[:, :], octs_by_tile[:, :, 1], 256.0, octs_by_tile[:, :, 0], ALU.mult, ALU.add).then_inc(bounds_ok, 1)
            dve.wait_ge(bounds_ok, 3)
            next_octs = first_oct[:, 1:NT + 1].rearrange("p (g j) -> p g j", j=2)
            V.scalar_tensor_tensor(turns_f[:, :], next_octs[:, :, 1], 65536.0, turns_f[:, :], ALU.mult, ALU.add).then_inc(bounds_ok, 1)
            dve.wait_ge(bounds_ok, 4)
            V.tensor_copy(turns_i[:, :], turns_f[:, :]).then_inc(bounds_ok, 1)
            dve.wait_ge(bounds_ok, 5)

            def high_part(b, i, waits):
                dve.wait_ge(xc_ok, b * 2 + (i + 1))
                if waits:
                    dve.wait_ge(table_out[i], b * 16)
                V.tensor_copy(hl[:, i, HI_ACT:LT, 0, :], xc[:, i, HI_ACT:LT, :]).then_inc(hi_ok, 1)

            def norm_turn(b, i):
                k = b * 2 + (i + 1)
                for part, loaded in ((FIRST, x_in[i][0]), (REST, x_in[i][1])):
                    dve.wait_ge(loaded, b * 16 + 16)
                    for t in range(part.start, part.stop):
                        ins = V.bn_stats(stats[:, t, :], xin[:, i, t, :])
                ins.then_inc(stats_ok, 1)
                dve.wait_ge(stats_ok, k)
                dve.sem_inc(stats_seen, 1)
                for t in range(LT):
                    ins = V.bn_aggr(mv[:, t, :], stats[:, t, :])
                ins.then_inc(var_ok, 1)
                dve.wait_ge(var_ok, k)
                newton_steps = Chain(dve, newton_chain, (b * 2 + i) * 4)
                var, mean = mv[:, :, 1], mv[:, :, 0]
                newton_steps.link(V.tensor_scalar(newton[:, 0, :], var, EPS, -0.5 / S_X ** 2, ALU.add, ALU.mult))
                if i == 1:
                    high_part(b, 0, not (isinstance(b, int) and b == 0))
                elif not (isinstance(b, int) and b == 0):
                    high_part(b - 1, 1, not (isinstance(b, int) and b == 1))
                dve.wait_ge(guess_ok, k)
                newton_steps.link(V.tensor_tensor(newton[:, 1, :], guess[:, :], guess[:, :], ALU.mult))
                newton_steps.link(V.tensor_tensor(newton[:, 1, :], newton[:, 1, :], newton[:, 0, :], ALU.mult))
                newton_steps.link(V.scalar_tensor_tensor(slope[:, :], newton[:, 1, :], 1.5, guess[:, :], ALU.add, ALU.mult))
                V.scalar_tensor_tensor(shift[:, :], mean, -1.0, slope[:, :], ALU.mult, ALU.mult).then_inc(affine_ok, 1)
            for b in range(2):
                norm_turn(b, 0)
                norm_turn(b, 1)
            with dve.Fori(2, LTURNS // 2) as b:
                norm_turn(b, 0)
                norm_turn(b, 1)
            high_part(LTURNS // 2 - 1, 1, True)

            def rest(n, to, frm, hi):
                dve.wait_ge(stage_hi, n)
                V.scalar_tensor_tensor(to, frm, S_W, hi, ALU.mult, ALU.subtract).then_inc(stage_lo, 1)

            rest(1, gnn_w[:, 1], stage[:, 0:2 * KC], gnn_w[:, 0])
            rest(2, rw1[:, 1], stage[:, 2 * KC:3 * KC, 0:P], rw1[:, 0])
            for n in range(3):
                rest(3 + n, ew[n][:, 1], stage[:, :, :], ew[n][:, 0])
            dve.wait_ge(small_in, 16 * 9)
            dve.wait_ge(bias_ok, 6)
            V.scalar_tensor_tensor(rw2_s[:, 1, :], rw2[:, :], S_W, rw2_s[:, 0, :], ALU.mult, ALU.subtract).then_inc(small_lo, 1)
            mid = slice(STACK, STACK + EXPERTS)
            V.scalar_tensor_tensor(eb3_s[mid, :], eb3[mid, :], S_W, eb3_s[mid, :], ALU.mult, ALU.subtract).then_inc(small_lo, 1)

            def one_hots(n1, j, q):
                v1 = dve.snap(q + n1)
                for half in range(2):
                    dve.wait_ge(hot_free[half], v1)
                    V.tensor_tensor(hot[:, half], ids[:, j, :].unsqueeze(1).to_broadcast([P, HOT, P]),
                                    dst_col[:, bass.ds(q * OCT + half * HOT, HOT)].unsqueeze(2).to_broadcast([P, HOT, P]),
                                    ALU.is_equal).then_inc(hot_ready[half], 1)

            def more_one_hots(n1, j, first_q, last_q):
                with dve.If(first_q < last_q):
                    with dve.Fori(first_q + 1, last_q + 1) as q:
                        one_hots(n1, j, q)

            def routing_picks(g):
                route = Chain(dve, route_chain, g * 14 + 8)
                dve.wait_ge(egap_ok, g + 1)
                route.link(V.tensor_scalar(w12[:, :, 0], egap[:, :], 1.0, None, ALU.add))
                route.link(V.reciprocal(w12[:, :, 0], w12[:, :, 0]))
                route.link(V.tensor_tensor(w12[:, :, 1], w12[:, :, 0], egap[:, :], ALU.mult))
                for j in range(2):
                    for c in range(2):
                        ins = V.tensor_scalar(pick[:, c, j, :], iota_f[:, 0:EXPERTS], best_f[:, j, c:c + 1], w12[:, j, c:c + 1], ALU.is_equal, ALU.mult)
                ins.then_inc(route_chain, 1)

            def routing_weights(g):
                dve.wait_ge(route_chain, g * 14 + 12)
                route = Chain(dve, route_chain, g * 14 + 12)
                route.link(V.tensor_tensor(wsel[:, :, :], pick[:, 0], pick[:, 1], ALU.add))
                for n in range(2):
                    ins = V.tensor_scalar(wsel_p[:, :, n * STACK:n * STACK + EXPERTS], wsel[:, :, :], S_W, None, ALU.mult)
                route.link(ins)
                V.scalar_tensor_tensor(wsel_p[:, :, 2 * STACK:STACKED], wsel[:, :, :], S_W, wsel_p[:, :, 0:EXPERTS], ALU.mult, ALU.subtract).then_inc(w_ok, 1)
                V.tensor_scalar(wsel_s[:, :, :], wsel[:, :, :], 1.0 / (S_H * S_W), None, ALU.mult).then_inc(ws_ok, 1)
                dve.wait_ge(ws_ok, g + 1)

            def iteration(g, front, ffn, more):
                g1 = g + 1 if isinstance(g, int) else dve.snap(g + 1)
                f6 = (g - 1) * EXPERTS if isinstance(g, int) else dve.snap((g - 1) * EXPERTS)

                def low(e, tmp, tmp_ok, hid, hi_part, lo_part):
                    dve.wait_ge(hi_part, f6 + (e + 1))
                    V.tensor_tensor(hid[:, e % 2, 1], tmp[:, e % 2], hid[:, e % 2, 0], ALU.subtract).then_inc(lo_part, 1)

                def low1(e):
                    if ffn:
                        low(e, t1, t1_ok, h1, h1h_ok, h1l_ok)

                def low2(e):
                    if ffn:
                        low(e, tmp2, t2_ok, h2, h2h_ok, h2l_ok)

                def combine(e):
                    if ffn:
                        dve.wait_ge(l3_done, f6 + (e + 1))
                        if e:
                            dve.wait_ge(acc_ok, f6 + e)
                        for j in range(2):
                            ins = V.scalar_tensor_tensor(acc[:, j, :], lay3[:, j * D:(j + 1) * D], wsel_s[:, j, e:e + 1],
                                                         acc[:, j, :], ALU.mult, ALU.add)
                        ins.then_inc(acc_ok, 1)

                low1(0)
                if ffn:
                    routing_picks(g - 1)
                if front:
                    dve.wait_ge(seg_done, g1 * 2)
                    V.tensor_scalar(rdeg[:, :], bank_x[:, DEG:DEG + 2], 1.0, None, ALU.max).then_inc(deg_ok, 1)
                    dve.wait_ge(deg_ok, g1)
                    V.reciprocal(rdeg[:, :], rdeg[:, :]).then_inc(rdeg_ok, 1)
                if ffn:
                    routing_weights(g - 1)
                if front:
                    for j in range(2):
                        dve.wait_ge(aggh_scaled, g * 2 + (j + 1))
                        V.scalar_tensor_tensor(agg[:, j, :], seg[j][:, D:2 * D], rdeg[:, j:j + 1], agg[:, j, :], ALU.mult, ALU.add).then_inc(agg_ok, 1)
                if front:
                    dve.wait_ge(x2_in, g1 * 16)
                    V.tensor_tensor(xb[:, :, :], x2[:, :, :], bself[:, :].unsqueeze(1).to_broadcast([P, 2, D]), ALU.add).then_inc(xb_ok, 1)
                low1(1)
                if ffn:
                    dve.wait_ge(b3_done, g)
                    V.scalar_tensor_tensor(acc[:, :, :].rearrange("p j d -> p (j d)"), bank_z[:, :], 1.0 / S_W ** 2,
                                           h[:, :, :].rearrange("p j d -> p (j d)"), ALU.mult, ALU.add).then_inc(acc0_ok, 1)
                if front:
                    dve.wait_ge(aggh_ok, g1)
                    V.tensor_tensor(agg_t[:, 1].rearrange("p k t -> p (k t)"), bank_y[:, :], agg_t[:, 0].rearrange("p k t -> p (k t)"), ALU.subtract).then_inc(aggl_ok, 1)
                    V.tensor_scalar(ids[:, :, :], ids[:, :, :], float(TOK), None, ALU.add).then_inc(ids_ok, 1)
                    dve.wait_ge(ids_ok, g + 3)
                low2(0)
                low1(2)
                if front:
                    dve.wait_ge(gnn_done, g1)
                    dve.wait_ge(xb_ok, g1)
                    V.scalar_tensor_tensor(h[:, :, :].rearrange("p j d -> p (j d)"), bank_z[:, :], 1.0 / (S_X * S_W),
                                           xb[:, :, :].rearrange("p j d -> p (j d)"), ALU.mult, ALU.add).then_inc(h_ok, 1)
                    dve.wait_ge(h_ok, g1)
                    for j in range(2):
                        ins = V.bn_stats(stats2[:, j, :], h[:, j, :])
                    ins.then_inc(stats2_ok, 1)
                    dve.wait_ge(stats2_ok, g1)
                    dve.sem_inc(stats_seen, 1)
                    for j in range(2):
                        ins = V.bn_aggr(mv2[:, j, :], stats2[:, j, :])
                    ins.then_inc(var2_ok, 1)
                low2(1)
                if ffn:
                    dve.wait_ge(acc0_ok, g)
                combine(0)
                low1(3)
                if front:
                    dve.wait_ge(var2_ok, g1)
                    n2 = Chain(dve, newton2_chain, g * 4)
                    n2.link(V.tensor_scalar(newton2[:, 0, :], mv2[:, :, 1], EPS, -0.5 / S_X ** 2, ALU.add, ALU.mult))
                    dve.wait_ge(guess2_ok, g1)
                    n2.link(V.tensor_tensor(newton2[:, 1, :], guess2[:, :], guess2[:, :], ALU.mult))
                    n2.link(V.tensor_tensor(newton2[:, 1, :], newton2[:, 1, :], newton2[:, 0, :], ALU.mult))
                    n2.link(V.scalar_tensor_tensor(rstd2[:, :], newton2[:, 1, :], 1.5, guess2[:, :], ALU.add, ALU.mult))
                    for j in range(2):
                        ins = V.tensor_scalar(y[:, j, :], h[:, j, :], mv2[:, j, 0:1], rstd2[:, j:j + 1], ALU.subtract, ALU.mult)
                    ins.then_inc(y_ok, 1)
                low2(2)
                combine(1)
                low1(4)
                low2(3)
                low1(5)
                if front:
                    dve.wait_ge(yh_ok, g1)
                    V.tensor_tensor(y_t[:, 1].rearrange("p k t -> p (k t)"), bank_y[:, :], y_t[:, 0].rearrange("p k t -> p (k t)"), ALU.subtract).then_inc(yl_ok, 1)
                combine(2)
                if more:
                    turns = turns_of(dve, g + 1)
                    n1, n2 = g * 2 + 3, g * 2 + 4
                    if not isinstance(g, int):
                        n1, n2 = dve.snap(n1), dve.snap(n2)
                    one_hots(n1, 0, turns[0])
                low2(4)
                if front:
                    dve.wait_ge(rhh_ok, g1)
                    V.tensor_tensor(rh_s[:, 1, :], rh[:, :], rh_s[:, 0, :], ALU.subtract).then_inc(rhl_ok, 1)
                combine(3)
                if front:
                    route = Chain(dve, route_chain, g * 14)
                    dve.wait_ge(logit_done, g1)
                    route.link(V.scalar_tensor_tensor(logit[:, :, :], bank_x[:, TOK:TOK + 2 * EXPERTS].rearrange("p (j e) -> p j e", j=2),
                                                      1.0 / (S_H * S_W), rb2[:, :].unsqueeze(1).to_broadcast([P, 2, EXPERTS]), ALU.mult, ALU.add))
                    route.link(V.tensor_reduce(top[:, :], logit[:, :, :], AX_X, ALU.max))
                    V.tensor_tensor(logit[:, :, :], logit[:, :, :], top[:, :].unsqueeze(2).to_broadcast([P, 2, EXPERTS]), ALU.subtract).then_inc(shifted_ok, 1)
                combine(4)
                if more:
                    more_one_hots(n1, 0, turns[0], turns[1])
                low2(5)
                if more:
                    one_hots(n2, 1, turns[1])
                if front:
                    dve.wait_ge(expo_ok, g1)
                    route.link(V.tensor_reduce(total[:, :], expo[:, :, :], AX_X, ALU.add))
                    route.link(V.reciprocal(total[:, :], total[:, :]))
                    route.link(V.tensor_tensor(prob[:, :, 0:EXPERTS], expo[:, :, :], total[:, :].unsqueeze(2).to_broadcast([P, 2, EXPERTS]), ALU.mult))
                    dve.sem_inc(stats_seen, 1)
                    for j in range(2):
                        ins = V.max(best[:, j, :], prob[:, j, :])
                    route.link(ins)
                    V.tensor_tensor(gap[:, :], best[:, :, 1], best[:, :, 0], ALU.subtract).then_inc(gap_ok, 1)
                    for j in range(2):
                        ins = V.max_index(best_i[:, j, :], best[:, j, :], prob[:, j, :])
                    route.link(ins)
                    route.link(V.tensor_copy(best_f[:, :, 0:2], best_i[:, :, 0:2]))
                combine(5)
                if more:
                    more_one_hots(n2, 1, turns[1], turns[2])

            turns = turns_of(dve, 0)
            for j in range(2):
                one_hots(j + 1, j, turns[j])
                more_one_hots(j + 1, j, turns[j], turns[j + 1])
            iteration(0, True, False, True)
            with dve.Fori(1, GROUPS - 1) as g:
                iteration(g, True, True, True)
            iteration(GROUPS - 1, True, True, False)
            iteration(GROUPS, False, True, False)


_INS = ["x", "src", "dst", "L0_gnn_W_neigh", "L0_gnn_W_self", "L0_gnn_b_self", "L0_ffn_router_w1", "L0_ffn_router_b1",
        "L0_ffn_router_w2", "L0_ffn_router_b2", "L0_ffn_expert_w1", "L0_ffn_expert_b1", "L0_ffn_expert_w2",
        "L0_ffn_expert_b2", "L0_ffn_expert_w3", "L0_ffn_expert_b3"]


def kernel(**inputs):
    import numpy as _np
    import concourse.bacc as _bacc
    from concourse import mybir as _mybir
    from concourse.bass_utils import run_bass_kernel_spmd as _run

    nc = _bacc.Bacc("TRN2", target_bir_lowering=False, num_devices=1)
    arrays, args = {}, []
    for name in _INS:
        a = _np.asarray(inputs[name])
        if name == "x":
            a = _np.pad(a, ((0, NT * P - N), (0, 0)))
        elif name in ("src", "dst"):
            a = _np.pad(a, (0, ST * P * P - EDGES), constant_values=1 << 20 if name == "dst" else 0).reshape(ST * P, P)
        elif name in ("L0_gnn_W_neigh", "L0_gnn_W_self"):
            a = a.T
        a = _np.ascontiguousarray(a)
        arrays[f"in_{name}_dram"] = a
        args.append(nc.dram_tensor(f"in_{name}_dram", a.shape, _mybir.dt.from_np(a.dtype), kind="ExternalInput").ap())
    args.append(nc.dram_tensor("out_0_dram", (NT * P, D), _mybir.dt.from_np(_np.dtype("float32")), kind="ExternalOutput").ap())
    build(nc, *args)
    r = _run(nc, [arrays], core_ids=[0])
    return r.results[0]["out_0_dram"][:N]
```
